# Optimizing a Trainium2 kernel written in Bass

```python
import numpy as np
import jax
import jax.numpy as jnp

def _softmax(x, axis=-1):
    return jax.nn.softmax(x, axis=axis)

def _gelu(x):
    return jax.nn.gelu(x, approximate=True)

def _silu(x):
    return jax.nn.silu(x)

def _sigmoid(x):
    return jax.nn.sigmoid(x)

def _layernorm(x, axis=-1, eps=1e-05):
    m = jnp.mean(x, axis=axis, keepdims=True)
    v = jnp.var(x, axis=axis, keepdims=True)
    return (x - m) / jnp.sqrt(v + eps)

def _scatter_add(tgt, idx, src, axis=0):
    return tgt.at[idx].add(src)

def _segment_sum(src, seg, n):
    return jax.ops.segment_sum(src, seg, n)
kernel_name = 'mk_rec_standalone_d1_rec_r8_484a01'

def setup_inputs(seed: int=0):
    np.random.seed(seed)
    _w = jnp.asarray

    def _rec_inputs():
        import jax
        import jax.numpy as jnp
        _rk = jax.random.key(seed)
        r_user_idx = jax.random.randint(jax.random.fold_in(_rk, 1), (512,), 176, 99964, jnp.int32)
        r_context_idx = jnp.stack([jax.random.randint(jax.random.fold_in(jax.random.fold_in(_rk, 2), 0), (512,), 69, 99837, jnp.int32), jax.random.randint(jax.random.fold_in(jax.random.fold_in(_rk, 2), 1), (512,), 134, 99935, jnp.int32), jax.random.randint(jax.random.fold_in(jax.random.fold_in(_rk, 2), 2), (512,), 67, 99938, jnp.int32)], axis=1)
        return (r_user_idx, r_context_idx)
    r_user_idx, r_context_idx = _rec_inputs()

    def _L0_rec_setup():
        import jax, jax.numpy as jnp
        import numpy as np
        NEG_SLOPE = 0.2

        def gat_conv(x, src, dst, W, att_src, att_dst, bias, heads):
            N = x.shape[0]
            Fout = att_src.shape[-1]
            h = (x @ W).reshape(N, heads, Fout)
            a_s = jnp.einsum('nhc,hc->nh', h, att_src)
            a_d = jnp.einsum('nhc,hc->nh', h, att_dst)
            e = jax.nn.leaky_relu(a_s[src] + a_d[dst], NEG_SLOPE)
            m = jax.lax.stop_gradient(jax.ops.segment_max(e, dst, num_segments=N))
            ex = jnp.exp(e - m[dst])
            denom = jax.ops.segment_sum(ex, dst, num_segments=N)
            alpha = ex / (denom[dst] + 1e-16)
            msg = h[src] * alpha[:, :, None]
            out = jax.ops.segment_sum(msg, dst, num_segments=N)
            return out.reshape(N, heads * Fout) + bias
        key = jax.random.key(seed)
        ks = jax.random.split(key, 16)
        NU, NS, D, H, CTX, B, E = (12500, 12500, 64, 2, 3, 512, 200000)
        inp = {'user_idx': jax.random.randint(ks[0], (B,), 0, NU), 'context_idx': jax.random.randint(ks[1], (B, CTX), 0, NS), 'edge_index': jax.random.randint(ks[2], (2, E), 0, NS), 'user_emb': jax.random.normal(ks[3], (NU, D), jnp.float32), 'service_emb': jax.random.normal(ks[4], (NS, D), jnp.float32), 'W1': jax.random.normal(ks[5], (D, H * D), jnp.float32) / np.sqrt(D), 'att_src1': jax.random.normal(ks[6], (H, D), jnp.float32) / np.sqrt(D), 'att_dst1': jax.random.normal(ks[7], (H, D), jnp.float32) / np.sqrt(D), 'b1': jnp.zeros((H * D,), jnp.float32), 'W2': jax.random.normal(ks[8], (H * D, D), jnp.float32) / np.sqrt(H * D), 'att_src2': jax.random.normal(ks[9], (1, D), jnp.float32) / np.sqrt(D), 'att_dst2': jax.random.normal(ks[10], (1, D), jnp.float32) / np.sqrt(D), 'b2': jnp.zeros((D,), jnp.float32), 'fc_w': jax.random.normal(ks[11], (D * (CTX + 1), NS), jnp.float32) / np.sqrt(D * (CTX + 1)), 'fc_b': jnp.zeros((NS,), jnp.float32)}
        return inp
    _L0_rec_all = _L0_rec_setup()
    _L0_rec_in = {k: v for k, v in _L0_rec_all.items() if k in ('edge_index', 'user_emb', 'service_emb', 'W1', 'att_src1', 'att_dst1', 'b1', 'W2', 'att_src2', 'att_dst2', 'b2', 'fc_w', 'fc_b')}
    del _L0_rec_all
    return {'r_user_idx': r_user_idx, 'r_context_idx': r_context_idx, 'L0_rec_edge_index': _L0_rec_in['edge_index'], 'L0_rec_user_emb': _L0_rec_in['user_emb'], 'L0_rec_service_emb': _L0_rec_in['service_emb'], 'L0_rec_W1': _L0_rec_in['W1'], 'L0_rec_att_src1': _L0_rec_in['att_src1'], 'L0_rec_att_dst1': _L0_rec_in['att_dst1'], 'L0_rec_b1': _L0_rec_in['b1'], 'L0_rec_W2': _L0_rec_in['W2'], 'L0_rec_att_src2': _L0_rec_in['att_src2'], 'L0_rec_att_dst2': _L0_rec_in['att_dst2'], 'L0_rec_b2': _L0_rec_in['b2'], 'L0_rec_fc_w': _L0_rec_in['fc_w'], 'L0_rec_fc_b': _L0_rec_in['fc_b']}

def reference(r_user_idx, r_context_idx, L0_rec_edge_index, L0_rec_user_emb, L0_rec_service_emb, L0_rec_W1, L0_rec_att_src1, L0_rec_att_dst1, L0_rec_b1, L0_rec_W2, L0_rec_att_src2, L0_rec_att_dst2, L0_rec_b2, L0_rec_fc_w, L0_rec_fc_b):
    import jax
    import jax.numpy as jnp

    def _L0_rec_ref(user_idx, context_idx, edge_index, user_emb, service_emb, W1, att_src1, att_dst1, b1, W2, att_src2, att_dst2, b2, fc_w, fc_b):
        import jax, jax.numpy as jnp
        import numpy as np
        NEG_SLOPE = 0.2

        def gat_conv(x, src, dst, W, att_src, att_dst, bias, heads):
            N = x.shape[0]
            Fout = att_src.shape[-1]
            h = (x @ W).reshape(N, heads, Fout)
            a_s = jnp.einsum('nhc,hc->nh', h, att_src)
            a_d = jnp.einsum('nhc,hc->nh', h, att_dst)
            e = jax.nn.leaky_relu(a_s[src] + a_d[dst], NEG_SLOPE)
            m = jax.lax.stop_gradient(jax.ops.segment_max(e, dst, num_segments=N))
            ex = jnp.exp(e - m[dst])
            denom = jax.ops.segment_sum(ex, dst, num_segments=N)
            alpha = ex / (denom[dst] + 1e-16)
            msg = h[src] * alpha[:, :, None]
            out = jax.ops.segment_sum(msg, dst, num_segments=N)
            return out.reshape(N, heads * Fout) + bias
        N = service_emb.shape[0]
        loops = jnp.arange(N)
        src = jnp.concatenate([edge_index[0], loops])
        dst = jnp.concatenate([edge_index[1], loops])
        user_vec = user_emb[user_idx]
        g = gat_conv(service_emb, src, dst, W1, att_src1, att_dst1, b1, heads=2)
        g = jax.nn.elu(g)
        g = gat_conv(g, src, dst, W2, att_src2, att_dst2, b2, heads=1)
        ctx = g[context_idx]
        ctx = ctx.reshape(ctx.shape[0], -1)
        x = jnp.concatenate([user_vec, ctx], axis=1)
        return x @ fc_w + fc_b
    y = _L0_rec_ref(r_user_idx, r_context_idx, L0_rec_edge_index, L0_rec_user_emb, L0_rec_service_emb, L0_rec_W1, L0_rec_att_src1, L0_rec_att_dst1, L0_rec_b1, L0_rec_W2, L0_rec_att_src2, L0_rec_att_dst2, L0_rec_b2, L0_rec_fc_w, L0_rec_fc_b)
    return y

_drawn_inputs = setup_inputs


def setup_inputs(seed=0):
    import zlib

    import numpy as np

    out = dict(_drawn_inputs(seed))
    spreads = {'L0_rec_b1': (0.0, 0.1), 'L0_rec_b2': (0.0, 0.1), 'L0_rec_fc_b': (0.0, 0.1)}
    factors = {'L0_rec_att_src2': 3.295, 'L0_rec_att_dst2': 5.736}
    for name, (base, spread) in spreads.items():
        noise = np.random.default_rng([zlib.crc32(name.encode()), seed]).standard_normal(out[name].shape)
        drawn = base * np.exp(spread * noise) if base else spread * noise
        out[name] = jnp.asarray(drawn.astype(out[name].dtype))
    for name, factor in factors.items():
        out[name] = (out[name] * factor).astype(out[name].dtype)
    return out
```

```python
from contextlib import ExitStack

import concourse.bass as bass
import concourse.mybir as mybir
import numpy as np
from concourse.alu_op_type import AluOpType as ALU

F32, BF16, F16 = mybir.dt.float32, mybir.dt.bfloat16, mybir.dt.float16
I32, U8 = mybir.dt.int32, mybir.dt.uint8
ACT = mybir.ActivationFunctionType
AX = mybir.AxisListType

P = 128
LO = 32
GROUPS = P // LO
WORD = 24
PARTS = 3
TAGGED = 0x20000000
HALF = 8
RANKS = 64
NBK = 12
CAP = NBK * P
SLOPE = 0.2
TINY = 1e-16
NEG = -1.0e30
NONE = 16383.0
KEYBITS = 14


class Tally:

    def __init__(self, eng, sem, name, first, step):
        self.eng, self.sem, self.first, self.step = eng, sem, first, step
        self.reg = eng.alloc_register(name)
        self.restart()

    def restart(self):
        self.eng.reg_mov(self.reg, self.first)

    def wait(self):
        self.eng.wait_ge(self.sem, self.reg)
        self.eng.reg_add(self.reg, self.reg, self.step)


def graph_kernel(nc, user_idx, context_idx, edge_index, user_emb, service_emb, W1, att_src1, att_dst1,
                 b1, W2, att_src2, att_dst2, b2, fc_w, fc_b, out):
    E = edge_index.shape[1]
    N, D = service_emb.shape
    NU = user_emb.shape[0]
    B, CTX = context_idx.shape
    H = att_src1.shape[0]
    NOUT = fc_w.shape[1]
    HI = -(-(-(-N // LO)) // WORD) * WORD
    NW = HI // WORD
    EP = E // P
    REST = E - EP * P
    TL = 392
    T = GROUPS * TL
    BANK = 7
    STEP = 2 * BANK
    STEPS = TL // STEP
    assert EP + 1 <= T and TL % (2 * STEP) == 0 and GROUPS * NW * BANK <= 512 and LO * HI < 1 << KEYBITS
    assert H * D == P and HI <= 512 and B % P == 0
    GPW = GROUPS * NW
    ROW1, ROW2 = D + 2 * H, D + 2
    BQ = B // P
    CQ = BQ * CTX
    PN, XC = 125, 20
    XT = N // PN
    NEVER = LO * HI - 1
    assert PN * XT == N and XT % XC == 0 and XC % 4 == 0 and N < (1 << KEYBITS) - 1 and NEVER >= N
    ZW = 200
    assert XT * ROW2 % ZW == 0 and XT * D % ZW == 0
    SCW, NCW = 2500, 500
    assert NOUT % SCW == 0

    with ExitStack() as ctx:
        ctx.enter_context(nc.allow_low_precision(reason="sums of integers below 2 ** 24, as int32"))

        def sb(name, shape, dt=F32):
            return ctx.enter_context(nc.sbuf_tensor(name, shape, dt))

        def sem(name):
            return ctx.enter_context(nc.semaphore(name))

        def dram(name, shape, dt):
            return nc.dram_tensor(name, shape, dt).ap()

        lo_d = dram("lo_rows", [GROUPS, P * TL], BF16)
        num_d = dram("target_numbers", [LO * HI, 1], I32)
        tab1_d = dram("table1", [1 + N, ROW1], F32)
        tab2_d = dram("table2", [1 + N, ROW2], F32)
        routed_d = dram("routed2", [P, HALF * RANKS], F32)
        g2_d = dram("layer2_rows", [1 + N, D], F32)
        list_d = dram("edge_lists2", [3, P, T], I32)

        big = sb("big", [P, TL * P], BF16)
        onehot_lo = big[:, :].rearrange("q (p t) -> q p t", p=P)
        fcw = big[:, 0:2 * 2 * NOUT].bitcast(F32).rearrange("p (k n) -> p k n", k=2)
        OHJ = T * NW // 4
        share = sb("share", [P, OHJ + 6 * T], F32)
        l_val = share[:, 0:T].bitcast(I32)
        l_clo = share[:, T:2 * T].bitcast(I32)
        wordf = share[:, T:2 * T]
        l_rank = share[:, 2 * T:3 * T].bitcast(I32)
        prods = [share[:, s * 2 * BANK * GPW:(s + 1) * 2 * BANK * GPW] for s in range(2)]
        packed = share[:, 3 * T:4 * T].bitcast(I32)
        bitpos = share[:, 4 * T:5 * T].bitcast(I32)
        keyf = share[:, 5 * T:6 * T]
        ohj = share[:, 6 * T:6 * T + OHJ].bitcast(U8)
        key = keyf.bitcast(I32)
        B0 = 3 * T - SCW
        bias = share[:, B0:B0 + NOUT]
        GAT = 2 * HALF * ROW1 + NBK * ROW1 + NBK * P
        WORK = HALF * P + 2 * HI + 2 * P
        gat_work = sb("gat_work", [P, max(GAT + WORK, 2 * SCW)])
        gat, work = gat_work[:, 0:GAT], gat_work[:, GAT:]
        rows = [gat[:, h * HALF * ROW1:(h + 1) * HALF * ROW1] for h in range(2)]
        o1 = 2 * HALF * ROW1
        node_rows = gat[:, o1:o1 + NBK * ROW1].rearrange("p (k r) -> p k r", k=NBK)
        acc_all = gat[:, o1 + NBK * ROW1:o1 + NBK * ROW1 + NBK * P].rearrange("p (k r) -> p k r", k=NBK)
        xchunk = [gat[:, i * XC * ROW1:(i + 1) * XC * ROW1].rearrange("p (t r) -> p t r", r=ROW1) for i in range(2)]
        ohc = [sb(f"ohc{h}", [P, HALF, P], BF16) for h in range(2)]
        ohk = [sb(f"ohk{h}", [P, HALF, NBK], BF16) for h in range(2)]
        o2 = o1 + NBK * ROW1
        assert o1 >= HALF * P and NBK >= HALF + HALF * RANKS // P
        ohcf = [gat[:, at:at + HALF * P] for at in (0, o2)]
        ohr0 = gat[:, o2 + HALF * P:o2 + HALF * P + HALF * RANKS].rearrange("p (c r) -> p c r", c=HALF)
        rankprod = work[:, 0:HALF * P]
        wprod = work[:, 0:H * HALF * D]
        ohr = work[:, 0:HALF * 3 * RANKS // 2].bitcast(BF16).rearrange("p (c q r) -> p c q r", c=HALF, q=3)
        gtmp, gtm2 = work[:, 0:HI], work[:, HI:2 * HI]
        w1_ = HALF * P
        routed = work[:, w1_:w1_ + HALF * RANKS]
        block = work[:, w1_ + HALF * RANKS:w1_ + 2 * HALF * RANKS]
        ohhi = work[:, w1_:w1_ + 2 * HI].bitcast(BF16).rearrange("p (c x) -> p c x", c=4)
        ohlo = work[:, w1_ + 2 * HI:w1_ + 2 * HI + 2 * P].bitcast(BF16).rearrange("p (c x) -> p c x", c=4)
        QB = 4
        hT, hpos, hneg = (work[:, k * QB * P:(k + 1) * QB * P] for k in range(3))
        srows = gat[:, o1:o1 + NBK * ROW2].rearrange("p (k r) -> p k r", k=NBK)
        stage = [gat_work[:, k * SCW:(k + 1) * SCW] for k in range(2)]
        xT = rankprod

        iota_hi = sb("iota_hi", [P, HI], F16)
        iota_p = sb("iota_p", [P, P], BF16)
        iota_lo = sb("iota_lo", [P, P], BF16)
        pidx = sb("pidx", [P, 1], I32)
        lane = sb("lane", [P, 1])
        pow2 = sb("pow2", [P, HI])
        onesf = sb("onesf", [P, 1])
        ident = sb("ident", [P, P])
        tri = sb("tri", [P, P], BF16)
        rtri = sb("rtri", [P, P], BF16)
        trib = sb("trib", [P, P], BF16)
        onesb = sb("onesb", [P, P], BF16)
        zerob = sb("zerob", [P, 512], BF16)
        numbers = sb("numbers", [P, HI])
        numi = sb("numi", [P, HI], I32)
        pow2i = numbers[:, :].bitcast(I32)
        words = sb("words", [P, PARTS, GPW], BF16)
        nodekey = sb("nodekey", [P, HI // GROUPS])
        naturals = sb("naturals", [P, HI], I32)

        gs = sb("gs", [P, 2])
        cnt = sb("cnt", [P, 4])
        cntb = sb("cntb", [P, 2], BF16)
        cntr = sb("cntr", [P, P])
        ci = sb("ci", [P, 16], I32)
        PASSES, ROUNDS, WINDOWS, PULLS, BLOCKS, AHEAD, NROUNDS, REROUTE = range(8)
        m8 = [sb(f"m8{h}", [P, HALF]) for h in range(2)]
        idx = [sb(f"idx{h}", [P, HALF], I32) for h in range(2)]
        vals = [sb(f"vals{h}", [P, HALF], I32) for h in range(2)]
        nums = [sb(f"nums{h}", [P, HALF], I32) for h in range(2)]
        w8 = sb("w8", [P, 8, HALF], I32)
        binb = sb("binb", [P, HALF], BF16)
        wf = sb("wf", [P, 8, HALF])
        nodelist = sb("nodelist", [P, NBK], I32)
        nodelist2 = sb("nodelist2", [P, NBK], I32)
        ci2 = sb("ci2", [P, 16], I32)
        sidx = sb("sidx", [P, 1], I32)
        sidx_all = sb("sidx_all", [P, NBK], I32)
        nodef = sb("nodef", [P, NBK])
        far = sb("far", [P, NBK])
        srow2 = sb("srow2", [P, D])
        lowk = sb("lowk", [P, 1])
        ad = sb("ad", [P, H])
        mx = sb("mx", [P, H])
        den = sb("den", [P, H])
        acc = sb("acc", [P, P])
        m_all = sb("m_all", [P, NBK, 2 * H])
        z = sb("z", [P, HALF, H])
        arg = sb("arg", [P, HALF + 1, H])
        pexp = sb("pexp", [P, HALF + 1, H])
        red2 = sb("red2", [P, H])
        mnew = sb("mnew", [P, H])
        wsum = sb("wsum", [P, P])
        w1 = sb("w1", [D, P])
        w1T = sb("w1T", [P, D])
        w1bd = sb("w1bd", [P, P])
        attbd = sb("attbd", [P, 2 * H])
        ua = sb("ua", [D, 2 * H])
        w2a = sb("w2a", [P, D + 2])
        w2T = sb("w2T", [D, P])
        att2 = sb("att2", [D, 2])
        b1c = sb("b1c", [P, 1])
        b2r = sb("b2r", [P, D])
        dummy = sb("dummy_row", [1, ROW1])
        cidx = sb("cidx", [P, CQ], I32)
        cidx1 = sb("cidx1", [P, CQ], I32)
        uidx = sb("uidx", [P, BQ], I32)
        wrapt = sb("wrapt", [P, CQ + BQ])
        wrapf = sb("wrapf", [P, CQ + BQ])
        xo = gat_work[:, SCW:SCW + BQ * D * (1 + CTX)].rearrange("p (q f) -> p q f", q=BQ)
        xoT = share[:, B0 + NOUT:B0 + NOUT + 2 * B].rearrange("p (k b) -> p k b", k=2)

        psf = ctx.enter_context(nc.psum_tensor("psf", [P, 4, 512], F32))
        psz = ctx.enter_context(nc.psum_tensor("psz", [P, HALF * P], F32))
        psm = ctx.enter_context(nc.psum_tensor("psm", [P, 512], F32))
        psd = ctx.enter_context(nc.psum_tensor("psd", [P, 512], F32))

        s_edges = sem("edges_loaded")
        s_small = sem("small_loaded")
        s_b2 = sem("b2_loaded")
        s_pads = sem("pads_set")
        s_zero = sem("weights_zeroed")
        s_const = sem("constants_built")
        s_lo = sem("lo_built")
        s_lost = sem("lo_stored")
        s_lobc = [sem(f"lo_broadcast{g}") for g in range(GROUPS)]
        s_x = [sem(f"x_loaded{i}") for i in range(2)]
        s_xst = [sem(f"table1_stored{i}") for i in range(2)]
        s_dum = sem("dummy_rows_stored")
        s_dumb = sem("dummy_row_built")
        s_xp = sem("pe_prepared")
        s_xa = sem("act_copied")
        s_ctx = sem("context_one_hots_built")
        s_ctxm = sem("context_marked")
        s_fd = sem("filter_products_done")
        s_ff = sem("filter_bank_free")
        s_idx = [sem(f"indices_ready{h}") for h in range(2)]
        s_num = [sem(f"numbers_gathered{h}") for h in range(2)]
        s_ohc = sem("bins_built")
        s_ohk = sem("blocks_built")
        s_ohcf = sem("bins_copied")
        s_ohr = sem("rank_values_built")
        s_z = sem("ranks_multiplied")
        s_rk = sem("ranks_read")
        s_mk = sem("marks_built")
        s_mm = sem("marks_multiplied")
        s_numb = sem("numbers_built")
        s_numst = sem("numbers_stored")
        s_pe = sem("pe_step")
        s_vp = sem("dve_step_for_pe")
        s_va = sem("dve_step_for_act")
        s_vg = sem("rows_for_pool")
        s_ac = sem("act_step")
        s_row = [sem(f"rows_gathered{h}") for h in range(2)]
        s_gi = [sem(f"row_indices_ready{h}") for h in range(2)]
        s_nrow = sem("node_row_gathered")
        s_ni = sem("nodes_back")
        s_list = sem("lists_saved")
        s_listb = sem("lists_back")
        s_st1 = sem("table2_rows_stored")
        s_st2 = sem("layer2_rows_stored")
        s_fcw = sem("fc_loaded")
        s_user = sem("user_rows_gathered")
        s_xrow = sem("context_rows_gathered")
        s_xt = sem("rows_transposed")
        s_xtc = sem("rows_transposed_in_sbuf")
        s_prod = sem("products_done")
        s_free = sem("product_bank_free")
        s_staged = [sem(f"out_staged{i}") for i in range(2)]
        s_out = [sem(f"out_stored{i}") for i in range(2)]

        tallies = {}

        def tally(eng_name, eng, s, name, first, step):
            tallies[(eng_name, name)] = Tally(eng, s, f"{eng_name}_{name}", first, step)

        def T_(eng_name, name):
            return tallies[(eng_name, name)]

        with nc.Block() as blk:
            @blk.gpsimd
            def _(pool):
                pool.memset(key[:, EP:T], NEVER).then_inc(s_pads, 1)
                pool.memset(packed[:, EP:T], 0).then_inc(s_pads, 1)
                pool.memset(attbd[:, :], 0.0).then_inc(s_zero, 1)
                pool.memset(w1bd[:, :], 0.0).then_inc(s_zero, 1)
                pool.memset(ident[:, :], 0.0)
                pool.memset(tri[:, :], 1.0)
                pool.memset(rtri[:, :], 1.0)
                pool.memset(trib[:, :], 1.0)
                pool.memset(onesb[:, :], 1.0)
                pool.memset(onesf[:, :], 1.0)
                pool.memset(zerob[:, :], 0.0)
                pool.iota(iota_hi[:, :], pattern=[[1, HI]], base=0, channel_multiplier=0, allow_small_or_imprecise_dtypes=True)
                pool.iota(iota_p[:, :], pattern=[[1, P]], base=0, channel_multiplier=0, allow_small_or_imprecise_dtypes=True)
                pool.iota(iota_lo[:, :], pattern=[[0, GROUPS], [1, LO]], base=0, channel_multiplier=0, allow_small_or_imprecise_dtypes=True)
                pool.iota(pidx[:, :], pattern=[[0, 1]], base=0, channel_multiplier=1)
                pool.iota(pow2i[:, :], pattern=[[0, NW], [1, WORD]], base=0, channel_multiplier=0)
                for g in range(GROUPS):
                    pool.drain()
                    pool.iota(naturals[g * LO:(g + 1) * LO, :], pattern=[[LO, HI]], base=1, channel_multiplier=1)
                pool.drain()
                pool.affine_select(out=ident[:, :], in_=ident[:, :], compare_op=ALU.not_equal, fill=1.0, base=0, pattern=[[-1, P]], channel_multiplier=1)
                pool.affine_select(out=tri[:, :], in_=tri[:, :], compare_op=ALU.is_gt, fill=0.0, base=0, pattern=[[1, P]], channel_multiplier=-1)
                pool.affine_select(out=rtri[:, :], in_=rtri[:, :], compare_op=ALU.is_ge, fill=0.0, base=0, pattern=[[-1, P]], channel_multiplier=1)
                for m in (trib, onesb):
                    v = m[:, :].rearrange("p (g e) -> p g e", g=GROUPS)
                    pool.affine_select(out=v, in_=v, compare_op=ALU.is_ge, fill=0.0, base=0, pattern=[[-LO, GROUPS], [0, LO]], channel_multiplier=1)
                pool.drain()
                pool.affine_select(out=trib[:, :], in_=trib[:, :], compare_op=ALU.is_gt, fill=0.0, base=0, pattern=[[1, P]], channel_multiplier=-1)
                v = onesb[:, :].rearrange("p (g e) -> p g e", g=GROUPS)
                pool.affine_select(out=v, in_=v, compare_op=ALU.is_ge, fill=0.0, base=LO - 1, pattern=[[LO, GROUPS], [0, LO]], channel_multiplier=-1)
                pool.memset(dummy[0:1, :], 0.0)
                pool.drain()
                pool.memset(dummy[0:1, D:D + H], NEG).then_inc(s_dumb, 1)
                pool.drain().then_inc(s_const, 1)
                tally("pool", pool, s_idx[0], "i0", 1, 1)
                tally("pool", pool, s_idx[1], "i1", 1, 1)
                tally("pool", pool, s_gi[0], "g0", 1, 1)
                tally("pool", pool, s_gi[1], "g1", 1, 1)
                tally("pool", pool, s_vg, "vg", 1, 1)

            @blk.sync
            def _(sp):
                sp.wait_ge(s_pads, 2)
                dst, src = edge_index[1], edge_index[0]
                sp.dma_start(key[:, 0:EP], dst[0:EP * P].rearrange("(p t) -> p t", p=P)).then_inc(s_edges, 16)
                sp.dma_start(packed[:, 0:EP], src[0:EP * P].rearrange("(p t) -> p t", p=P)).then_inc(s_edges, 16)
                with nc.allow_non_contiguous_dma(reason="one edge or weight of a partition"):
                    if REST:
                        sp.dma_start(key[0:REST, EP:EP + 1], dst[EP * P:E].rearrange("(p t) -> p t", t=1)).then_inc(s_edges, 16)
                        sp.dma_start(packed[0:REST, EP:EP + 1], src[EP * P:E].rearrange("(p t) -> p t", t=1)).then_inc(s_edges, 16)
                    sp.dma_start(cidx[:, :], context_idx.rearrange("(p q) c -> p (q c)", p=P)).then_inc(s_small, 16)
                    sp.dma_start(uidx[:, :], user_idx.rearrange("(p q) -> p q", p=P)).then_inc(s_small, 16)
                    sp.dma_start(w1[:, :], W1).then_inc(s_small, 16)
                    sp.wait_ge(s_zero, 2)
                    for h in range(H):
                        sp.dma_start(attbd[h * D:(h + 1) * D, h:h + 1], att_src1[h].rearrange("(p t) -> p t", t=1)).then_inc(s_small, 16)
                        sp.dma_start(attbd[h * D:(h + 1) * D, H + h:H + h + 1], att_dst1[h].rearrange("(p t) -> p t", t=1)).then_inc(s_small, 16)
                        sp.dma_start(w1bd[h * D:(h + 1) * D, h * D:(h + 1) * D], W1[:, h * D:(h + 1) * D]).then_inc(s_small, 16)
                    sp.dma_start(w2a[:, 0:D], W2).then_inc(s_small, 16)
                    sp.dma_start(att2[:, 0:1], att_src2[0].rearrange("(p t) -> p t", t=1)).then_inc(s_small, 16)
                    sp.dma_start(att2[:, 1:2], att_dst2[0].rearrange("(p t) -> p t", t=1)).then_inc(s_small, 16)
                    sp.dma_start(b1c[:, :], b1.rearrange("(p t) -> p t", t=1)).then_inc(s_small, 16)
                sp.dma_start(b2r[:, :], b2.rearrange("(o d) -> o d", o=1).to_broadcast([P, D])).then_inc(s_b2, 16)
                sp.wait_ge(s_lo, 1)
                sp.dma_start(lo_d.rearrange("g (p t) -> p g t", p=P),
                             l_val[:, 0:T // 2].bitcast(BF16).rearrange("p (g t) -> p g t", g=GROUPS)).then_inc(s_lost, 16)
                sp.wait_ge(s_lost, 16)
                for g in range(GROUPS):
                    sp.dma_start(big[g * LO:(g + 1) * LO, :], lo_d[g:g + 1, :].to_broadcast([LO, P * TL])).then_inc(s_lobc[g], 16)
                sp.wait_ge(s_dumb, 1)
                sp.dma_start(tab1_d[0:1, :], dummy[0:1, :]).then_inc(s_dum, 16)
                sp.dma_start(tab2_d[0:1, :], dummy[0:1, 0:ROW2]).then_inc(s_dum, 16)
                sp.wait_ge(s_const, 1)
                zf = zerob[:, :].bitcast(F32)
                for tab, w in ((tab2_d, ROW2), (g2_d, D)):
                    sp.dma_start(tab[1:1 + N, :].rearrange("(p a) r -> p (a r)", p=PN).rearrange("p (a z) -> p a z", z=ZW),
                                 zf[0:PN, 0:ZW].unsqueeze(1).to_broadcast([PN, XT * w // ZW, ZW])).then_inc(s_dum, 16)
                sp.dma_start(g2_d[0:1, :], zf[0:1, 0:D]).then_inc(s_dum, 16)
                sp.wait_ge(s_dum, 80)
                sp.wait_ge(s_b2, 16)

            NSMALL = 16 * (3 + 3 * H + 4)

            @blk.vector
            def _(v):
                v.wait_ge(s_small, NSMALL)
                v.tensor_copy(wrapf[:, 0:CQ], cidx[:, :])
                v.tensor_copy(wrapf[:, CQ:], uidx[:, :])
                v.drain()
                v.tensor_scalar(wrapt[:, 0:CQ], wrapf[:, 0:CQ], 0.0, float(N), ALU.is_lt, ALU.mult)
                v.tensor_scalar(wrapt[:, CQ:], wrapf[:, CQ:], 0.0, float(NU), ALU.is_lt, ALU.mult)
                v.drain()
                v.tensor_tensor(wrapf[:, :], wrapf[:, :], wrapt[:, :], ALU.add)
                v.drain()
                v.tensor_scalar(cidx[:, :], wrapf[:, 0:CQ], 0.0, float(N - 1), ALU.max, ALU.min)
                v.tensor_scalar(uidx[:, :], wrapf[:, CQ:], 0.0, float(NU - 1), ALU.max, ALU.min)
                v.wait_ge(s_edges, 64 if REST else 32)
                lo_i, hi_i = l_rank, l_clo
                v.tensor_scalar(lo_i[:, :], key[:, :], LO - 1, None, ALU.bitwise_and)
                v.tensor_scalar(hi_i[:, :], key[:, :], 5, None, ALU.arith_shift_right)
                v.drain()
                v.tensor_copy(l_val[:, 0:T // 2].bitcast(BF16), lo_i[:, :])
                v.tensor_scalar(packed[:, :], packed[:, :], 1.0, None, ALU.add)
                v.drain().then_inc(s_lo, 1)
                v.scalar_tensor_tensor(key[:, :], lo_i[:, :], float(HI), hi_i[:, :], ALU.mult, ALU.add)
                v.drain()
                v.tensor_scalar(lo_i[:, :], hi_i[:, :], 2731.0, None, ALU.mult)
                v.drain()
                v.tensor_scalar(lo_i[:, :], lo_i[:, :], 16, None, ALU.arith_shift_right)
                v.tensor_scalar(key[:, :], key[:, :], KEYBITS, TAGGED, ALU.logical_shift_left, ALU.bitwise_or)
                v.drain()
                v.scalar_tensor_tensor(bitpos[:, :], lo_i[:, :], -float(WORD), hi_i[:, :], ALU.mult, ALU.add)
                v.tensor_tensor(packed[:, :], packed[:, :], key[:, :], ALU.bitwise_or)
                v.drain()
                v.tensor_copy(wordf, lo_i[:, :])
                v.drain()
                v.wait_ge(s_const, 1)
                jv = wordf.rearrange("p (g t) -> p t g", g=GROUPS)
                ov = ohj[:, :].rearrange("p (t g j) -> p t g j", g=GROUPS, j=NW)
                for c in range(8):
                    w = TL // 8
                    v.tensor_tensor(
                        ov[:, c * w:(c + 1) * w],
                        jv[:, c * w:(c + 1) * w].unsqueeze(3).to_broadcast([P, w, GROUPS, NW]),
                        iota_p[:, 0:NW].unsqueeze(1).unsqueeze(1).to_broadcast([P, w, GROUPS, NW]), ALU.is_equal)
                v.tensor_scalar(pidx[:, :], pidx[:, :], LO - 1, None, ALU.bitwise_and)
                v.tensor_scalar(cidx1[:, :], cidx[:, :], 5, None, ALU.arith_shift_right)
                v.tensor_scalar(w8[:, 0:2, :].rearrange("p a b -> p (a b)")[:, 0:CQ], cidx[:, :], LO - 1, None, ALU.bitwise_and)
                v.drain()
                v.tensor_copy(lane[:, :], pidx[:, :])
                v.tensor_copy(wrapf[:, 0:CQ], cidx1[:, :])
                v.tensor_copy(wrapt[:, 0:CQ], w8[:, 0:2, :].rearrange("p a b -> p (a b)")[:, 0:CQ])
                v.memset(numi[:, :], 1)
                v.drain()
                v.tensor_tensor(pow2i[:, :], numi[:, :], pow2i[:, :], ALU.logical_shift_left)
                v.drain()
                v.tensor_copy(pow2[:, :], pow2i[:, :])
                v.tensor_scalar(cidx1[:, :], cidx[:, :], 1.0, None, ALU.add)
                for c0 in range(0, CQ, 4):
                    if c0:
                        v.wait_ge(s_ctxm, c0 // 4)
                    for c in range(4):
                        v.tensor_scalar(ohhi[:, c, :], iota_hi[:, :], wrapf[:, c0 + c:c0 + c + 1], None, ALU.is_equal)
                        v.tensor_scalar(ohlo[:, c, :], iota_lo[:, :], wrapt[:, c0 + c:c0 + c + 1], None, ALU.is_equal)
                    v.drain().then_inc(s_ctx, 1)
                for g in range(GROUPS):
                    v.wait_ge(s_lobc[g], 16)
                for c in range(8):
                    w = P // 8
                    part = onehot_lo[:, c * w:(c + 1) * w, :]
                    v.tensor_scalar(part, part, lane[:, 0:1], None, ALU.is_equal)
                tally("dve", v, s_fd, "fd", 1, 1)
                tally("dve", v, s_num[0], "num0", 16 * HALF, 16 * HALF)
                tally("dve", v, s_num[1], "num1", 16 * HALF, 16 * HALF)
                tally("dve", v, s_z, "z", 1, 1)
                tally("dve", v, s_mm, "mm", 1, 1)
                tally("dve", v, s_pe, "pe", 1, 1)
                tally("dve", v, s_ac, "ac", 1, 1)
                tally("dve", v, s_row[0], "row0", 16 * HALF, 16 * HALF)
                tally("dve", v, s_row[1], "row1", 16 * HALF, 16 * HALF)
                tally("dve", v, s_nrow, "nrow", 16 * NBK, 16 * NBK)
                tally("dve", v, s_st1, "st1", 16 * NBK, 16 * NBK)
                tally("dve", v, s_st2, "st2", 16, 16)

            @blk.scalar
            def _(act):
                def load(c):
                    act.dma_start(xchunk[c % 2][0:PN, :, 0:D],
                                  service_emb.rearrange("(p t) d -> p t d", p=PN)[:, c * XC:(c + 1) * XC, :]).then_inc(s_x[c % 2], 16)

                load(0)
                load(1)
                act.wait_ge(s_xp, 1)
                nc.scalar.copy(w1T[:, :], psd[:, 0:D])
                nc.scalar.copy(w2T[:, :], psd[0:D, 128:256])
                act.drain().then_inc(s_xa, 1)
                act.wait_ge(s_xp, 2)
                nc.scalar.copy(ua[:, :], psd[0:D, 256:256 + 2 * H])
                nc.scalar.copy(w2a[:, D:D + 2], psd[:, 272:274])
                act.drain().then_inc(s_xa, 1)
                step = 2
                for c in range(XT // XC):
                    for b in range(XC // 4):
                        act.wait_ge(s_xp, step + 1)
                        nc.scalar.copy(xT[0:D, 0:4 * PN], psf[0:D, b % 2, 0:4 * PN]).then_inc(s_xa, 1)
                        step += 1
                    act.wait_ge(s_xp, step + 1)
                    nc.scalar.copy(xchunk[c % 2][0:PN, :, D:ROW1],
                                   psf[0:PN, 2, 0:XC * 2 * H].rearrange("p (t k) -> p t k", t=XC)).then_inc(s_xa, 1)
                    step += 1
                    act.wait_ge(s_xa, step)
                    act.dma_start(tab1_d[1:1 + N, :].rearrange("(p t) r -> p t r", p=PN)[:, c * XC:(c + 1) * XC, :],
                                  xchunk[c % 2][0:PN]).then_inc(s_xst[c % 2], 16)
                    if c + 2 < XT // XC:
                        act.wait_ge(s_xst[c % 2], 16 * (c // 2 + 1))
                        load(c + 2)
                for i in range(2):
                    act.wait_ge(s_xst[i], 16 * ((XT // XC + 1 - i) // 2))
                tally("act", act, s_va, "va", 1, 1)
                tally("act", act, s_ohc, "ohc", 1, 1)

            @blk.tensor
            def _(pe):
                def mark_context():
                    for c0 in range(0, CQ, 4):
                        pe.wait_ge(s_ctx, c0 // 4 + 1)
                        for c in range(4):
                            last = nc.tensor.matmul(psm[:, 0:HI], ohlo[:, c, :], ohhi[:, c, :], start=(c0 + c == 0), stop=(c0 + c == CQ - 1), skip_group_check=True)
                        last.then_inc(s_ctxm, 1)

                pe.wait_ge(s_const, 1)
                pe.wait_ge(s_small, NSMALL)
                nc.tensor.transpose(psd[:, 0:D], w1[:, :], ident[0:D, 0:D])
                nc.tensor.transpose(psd[0:D, 128:256], w2a[:, 0:D], ident[:, :]).then_inc(s_xp, 1)
                pe.wait_ge(s_xa, 1)
                nc.tensor.matmul(psd[0:D, 256:256 + 2 * H], w1T[:, :], attbd[:, :], start=True, stop=True)
                nc.tensor.matmul(psd[:, 272:274], w2T[:, :], att2[:, :], start=True, stop=True).then_inc(s_xp, 1)
                pe.wait_ge(s_xa, 2)
                step = 2
                for c in range(XT // XC):
                    pe.wait_ge(s_x[c % 2], 16 * (c // 2 + 1))
                    for b in range(XC // 4):
                        for t in range(4):
                            last = nc.tensor.transpose(psf[0:D, b % 2, t * PN:(t + 1) * PN], xchunk[c % 2][0:PN, 4 * b + t, 0:D], ident[0:PN, 0:PN])
                        last.then_inc(s_xp, 1)
                        step += 1
                        pe.wait_ge(s_xa, step)
                        for t in range(4):
                            k = (4 * b + t) * 2 * H
                            last = nc.tensor.matmul(psf[0:PN, 2, k:k + 2 * H], xT[0:D, t * PN:(t + 1) * PN], ua[:, :], start=True, stop=True)
                    last.then_inc(s_xp, 1)
                    if c == 0:
                        mark_context()
                    step += 1
                    pe.wait_ge(s_xa, step)
                tally("pe", pe, s_ff, "ff", 1, 1)
                tally("pe", pe, s_ohc, "ohc", 1, 1)
                tally("pe", pe, s_rk, "rk", 1, 1)
                tally("pe", pe, s_ohk, "ohk", 1, 1)
                tally("pe", pe, s_ohcf, "ohcf", 1, 1)
                tally("pe", pe, s_ohr, "ohr", 1, 1)
                tally("pe", pe, s_mk, "mk", 1, 1)
                tally("pe", pe, s_vp, "vp", 1, 1)

        def to_count(v, column, target, shift, least=1, most=1 << 20):
            v.drain().then_inc(s_vp, 1)
            T_("dve", "pe").wait()
            v.tensor_reduce(cntr[0:1, 0:1], psd[0:1, 384:512], AX.X, ALU.max)
            v.drain()
            v.tensor_scalar(ci[0:1, 8:9], cntr[0:1, 0:1], float((1 << shift) - 1), None, ALU.add)
            v.drain()
            v.tensor_scalar(ci[0:1, 9:10], ci[0:1, 8:9], shift, None, ALU.arith_shift_right)
            v.drain()
            v.tensor_scalar(ci[0:1, target:target + 1], ci[0:1, 9:10], float(least), float(most), ALU.max, ALU.min)
            v.drain()

        def pe_count(pe, column):
            T_("pe", "vp").wait()
            nc.tensor.matmul(psd[0:1, 384:512], cnt[:, column:column + 1], ident[:, :], start=True, stop=True).then_inc(s_pe, 1)

        MAXPULLS = HALF * RANKS // (2 * HALF)

        def restart(name, sems):
            with nc.Block() as blk:
                @blk.gpsimd
                def _(pool):
                    pool.dma_reset(range(sems[0].num, sems[1].num + 1))
                    pool.sem_clear(range(sems[0].num, sems[1].num + 1))

                @blk.vector
                def _(v):
                    for h in range(2):
                        T_("dve", f"{name}{h}").restart()

        def sum_counts(m, at):
            for a in range(2):
                last = nc.tensor.matmul(psd[:, at:at + 1], m[:, :], cntb[:, a:a + 1], start=(a == 0), stop=(a == 1))
            return last

        def number_targets(times):
            with nc.Block() as blk:
                @blk.vector
                def _(v):
                    v.tensor_scalar(gtmp[:, :], psm[:, 0:HI], 0.0, None, ALU.is_gt)
                    v.memset(gs[:, 0:1], 0.0)
                    v.memset(gs[:, 1:2], float(CAP))
                    v.drain()
                    v.tensor_reduce(cntb[:, :], gtmp[:, :].rearrange("p (a b) -> p a b", a=2), AX.X, ALU.add)
                    v.drain().then_inc(s_vp, 1)
                    T_("dve", "pe").wait()
                    v.tensor_copy(cnt[:, 0:2], psd[:, 0:2])
                    v.drain()
                    v.tensor_tensor_scan(gtm2[:, :], onesf[:, :].to_broadcast([P, HI]), gtmp[:, :], cnt[:, 0:1], ALU.mult, ALU.add)
                    v.drain()
                    v.tensor_scalar(gtm2[:, :], gtm2[:, :], -1.0 - NONE, None, ALU.add)
                    v.drain()
                    v.tensor_tensor(gtm2[:, :], gtm2[:, :], gtmp[:, :], ALU.mult)
                    v.drain()
                    v.tensor_scalar(numbers[:, :], gtm2[:, :], NONE, None, ALU.add)
                    v.drain()
                    v.tensor_copy(numi[:, :], numbers[:, :])
                    v.drain().then_inc(s_numb, 1)
                    v.tensor_scalar(ci[0:1, 8:9], cnt[0:1, 1:2], float(CAP - 1), None, ALU.add)
                    v.drain()
                    v.tensor_scalar(ci[0:1, 9:10], ci[0:1, 8:9], 9, None, ALU.arith_shift_right)
                    v.drain()
                    v.tensor_scalar(ci[0:1, 8:9], ci[0:1, 9:10], 21846.0, None, ALU.mult)
                    v.drain()
                    v.tensor_scalar(ci[0:1, PASSES:PASSES + 1], ci[0:1, 8:9], 16, None, ALU.arith_shift_right)

                @blk.sync
                def _(sp):
                    sp.wait_ge(s_numb, times)
                    sp.dma_start(num_d.rearrange("(l h) o -> l (h o)", l=LO), numi[0:LO, :]).then_inc(s_numst, 16)
                    sp.wait_ge(s_numst, 16 * times)

                @blk.tensor
                def _(pe):
                    T_("pe", "vp").wait()
                    sum_counts(trib, 0)
                    sum_counts(onesb, 1).then_inc(s_pe, 1)

        def make_words():
            NK = HI // GROUPS
            with nc.Block() as blk:
                @blk.vector
                def _(v):
                    v.memset(words[:, :, :], 0.0)
                    v.tensor_scalar(gtmp[:, :], numbers[:, :], gs[:, 0:1], None, ALU.is_ge)
                    v.drain()
                    v.scalar_tensor_tensor(gtmp[:, :], numbers[:, :], gs[:, 1:2], gtmp[:, :], ALU.is_lt, ALU.mult)
                    v.drain()
                    v.tensor_tensor(gtm2[:, :], gtmp[:, :], pow2[:, :], ALU.mult)
                    v.drain()
                    v.tensor_reduce(cntr[:, 0:NW * PARTS], gtm2[:, :].rearrange("p (w b) -> p w b", b=WORD // PARTS), AX.X, ALU.add)
                    v.drain()
                    for g in range(GROUPS):
                        r = slice(g * LO, (g + 1) * LO)
                        v.tensor_copy(words[r, :, g * NW:(g + 1) * NW], cntr[r, 0:NW * PARTS].rearrange("p (w b) -> p b w", b=PARTS))
                    v.tensor_reduce(cntb[:, :], gtmp[:, :].rearrange("p (a b) -> p a b", a=2), AX.X, ALU.add)
                    v.tensor_scalar(gtm2[:, :].bitcast(I32), numi[:, :], KEYBITS, TAGGED, ALU.logical_shift_left, ALU.bitwise_or)
                    v.drain()
                    v.tensor_tensor(gtm2[:, :].bitcast(I32), gtm2[:, :].bitcast(I32), naturals[:, :], ALU.bitwise_or)
                    v.drain()
                    v.tensor_tensor(gtmp[:, :], gtmp[:, :], gtm2[:, :], ALU.mult)
                    v.drain()
                    for g in range(GROUPS):
                        r = slice(g * LO, (g + 1) * LO)
                        v.tensor_copy(nodekey[r, :], gtmp[r, g * NK:(g + 1) * NK])
                    v.drain()
                    v.tensor_scalar(block[:, 0:NK], nodekey[:, :], 0.0, None, ALU.is_gt)
                    v.drain()
                    v.tensor_reduce(cnt[:, 1:2], block[:, 0:NK], AX.X, ALU.add)
                    to_count(v, 1, NROUNDS, 3)
                    v.drain().then_inc(s_vp, 1)
                    T_("dve", "pe").wait()
                    v.tensor_copy(cnt[:, 2:3], psd[:, 1:2])
                    to_count(v, 2, BLOCKS, 7)

                @blk.tensor
                def _(pe):
                    pe_count(pe, 1)
                    T_("pe", "vp").wait()
                    sum_counts(onesb, 1).then_inc(s_pe, 1)
                    pe_count(pe, 2)

            with nc.Block() as blk:
                @blk.vector
                def _(v):
                    n = v.value_load(ci[0:1, NROUNDS:NROUNDS + 1], min_val=1, max_val=NK // HALF + 1)
                    with v.Fori(0, n) as _i:
                        v.max(m8[0][:, :], nodekey[:, :])
                        v.drain()
                        v.match_replace(nodekey[:, :], m8[0][:, :], nodekey[:, :], 0.0)
                        b8 = m8[0][:, :].bitcast(I32)
                        v.tensor_scalar(w8[:, 0, :], b8, KEYBITS, (1 << KEYBITS) - 1, ALU.logical_shift_right, ALU.bitwise_and)
                        v.tensor_scalar(w8[:, 1, :], b8, 127 << 7, None, ALU.bitwise_and)
                        v.tensor_scalar(w8[:, 2, :], b8, 127, None, ALU.bitwise_and)
                        v.drain()
                        v.tensor_scalar(w8[:, 3, :], w8[:, 0, :], gs[:, 0:1], None, ALU.subtract)
                        v.drain()
                        v.tensor_scalar(w8[:, 4, :], w8[:, 3, :], P - 1, None, ALU.bitwise_and)
                        v.tensor_scalar(w8[:, 5, :], w8[:, 3, :], 7, None, ALU.arith_shift_right)
                        v.drain()
                        v.tensor_copy(wf[:, 0:6, :], w8[:, 0:6, :])
                        v.drain()
                        for c in range(HALF):
                            v.tensor_scalar(ohc[0][:, c, :], iota_p[:, :], wf[:, 4, c:c + 1], None, ALU.is_equal)
                            for q in range(2):
                                v.tensor_scalar(ohr[:, c, q, 0:NBK], iota_p[:, 0:NBK], wf[:, 5, c:c + 1], wf[:, 1 + q, c:c + 1], ALU.is_equal, ALU.mult)
                        v.drain().then_inc(s_vp, 1)
                        T_("dve", "pe").wait()
                    v.tensor_copy(nodelist[:, :], psd[:, 0:NBK])

                @blk.tensor
                def _(pe):
                    nc.tensor.matmul(psd[:, 0:NBK], tri[:, :], zerob[:, 0:NBK], start=True, stop=False, skip_group_check=True)
                    n = pe.value_load(ci[0:1, NROUNDS:NROUNDS + 1], min_val=1, max_val=NK // HALF + 1)
                    with pe.Fori(0, n) as _i:
                        T_("pe", "vp").wait()
                        for c in range(HALF):
                            for q in range(2):
                                last = nc.tensor.matmul(psd[:, 0:NBK], ohc[0][:, c, :], ohr[:, c, q, 0:NBK], start=False, stop=False, skip_group_check=True)
                        last.then_inc(s_pe, 1)

        def gather_nodes(pool, table, row):
            for k in range(NBK):
                pool.indirect_dma_start(out=node_rows[:, k, 0:row], out_offset=None, in_=table,
                                        in_offset=bass.IndirectOffsetOnAxis(ap=nodelist[:, k:k + 1], axis=0)).then_inc(s_nrow, 16)

        def filter_edges(nodes):
            with nc.Block() as blk:
                if nodes:
                    @blk.gpsimd
                    def _(pool):
                        gather_nodes(pool, tab1_d, ROW1)

                @blk.tensor
                def _(pe):
                    with pe.Fori(0, STEPS // 2) as i:
                        for s in range(2):
                            T_("pe", "ff").wait()
                            for t in range(STEP):
                                for q in range(PARTS):
                                    last = nc.tensor.matmul(
                                        psf[:, 2 * s + t // BANK, (t % BANK) * GPW:(t % BANK + 1) * GPW],
                                        onehot_lo[:, :, bass.ds(i * (2 * STEP) + (s * STEP + t), 1)].rearrange("q p o -> q (p o)"),
                                        words[:, q, :], start=(q == 0), stop=(q == PARTS - 1))
                            last.then_inc(s_fd, 1)
                    T_("pe", "ff").wait()
                    T_("pe", "ff").wait()
                    pe_count(pe, 0)

                @blk.vector
                def _(v):
                    wv = key.rearrange("p (g t) -> p t g", g=GROUPS)
                    W2_ = BANK * GPW
                    for _k in range(2):
                        v.engine_nop().then_inc(s_ff, 1)
                    with v.Fori(0, STEPS // 2) as i:
                        for s in range(2):
                            T_("dve", "fd").wait()
                            v.tensor_tensor(prods[s].rearrange("p (b w) -> p b w", b=2), psf[:, 2 * s:2 * s + 2, 0:W2_],
                                            ohj[:, bass.ds(i * (4 * W2_) + s * 2 * W2_, 2 * W2_)].rearrange("p (b w) -> p b w", b=2), ALU.mult)
                            v.drain().then_inc(s_ff, 1)
                            v.tensor_reduce(wv[:, bass.ds(i * (2 * STEP) + s * STEP, STEP), :],
                                            prods[s].rearrange("p (t g j) -> p t g j", g=GROUPS, j=NW), AX.X, ALU.add)
                    v.drain()
                    v.tensor_tensor(key, key, bitpos, ALU.logical_shift_right)
                    v.drain()
                    v.tensor_scalar(key, key, 31, 31, ALU.logical_shift_left, ALU.arith_shift_right)
                    v.drain()
                    v.tensor_reduce(cnt[:, 1:3], key.rearrange("p (h t) -> p h t", h=2), AX.X, ALU.add, negate=True)
                    v.drain()
                    v.tensor_tensor(key, key, packed, ALU.bitwise_and)
                    v.tensor_tensor(cnt[:, 0:1], cnt[:, 1:2], cnt[:, 2:3], ALU.max)
                    to_count(v, 0, ROUNDS, 3)

        def compact_edges(mark_sources):
            restart("num", s_num)
            with nc.Block() as blk:
                @blk.gpsimd
                def _(pool):
                    n = pool.value_load(ci[0:1, ROUNDS:ROUNDS + 1], min_val=1, max_val=T // 16)
                    with pool.Fori(0, n) as _i:
                        for h in range(2):
                            T_("pool", f"i{h}").wait()
                            for c in range(HALF):
                                pool.indirect_dma_start(
                                    out=nums[h][:, c:c + 1], out_offset=None, in_=num_d,
                                    in_offset=bass.IndirectOffsetOnAxis(ap=idx[h][:, c:c + 1], axis=0)).then_inc(s_num[h], 16)
                    for h in range(2):
                        T_("pool", f"i{h}").wait()

                @blk.vector
                def _(v):
                    def pull(h):
                        part = keyf[:, h * T // 2:(h + 1) * T // 2]
                        v.max(m8[h][:, :], part)
                        v.drain()
                        b8 = m8[h][:, :].bitcast(I32)
                        v.tensor_scalar(vals[h][:, :], b8, (1 << KEYBITS) - 1, None, ALU.bitwise_and)
                        v.tensor_scalar(idx[h][:, :], b8, KEYBITS, (1 << KEYBITS) - 1, ALU.logical_shift_right, ALU.bitwise_and).then_inc(s_idx[h], 1)
                        v.match_replace(part, m8[h][:, :], part, 0.0)
                        v.drain()

                    def bins(h, at):
                        T_("dve", f"num{h}").wait()
                        v.tensor_scalar(w8[:, 0, :], nums[h][:, :], gs[:, 0:1], None, ALU.subtract)
                        v.tensor_scalar(w8[:, 1, :], vals[h][:, :], 0.0, 1024.0, ALU.is_equal, ALU.mult)
                        v.drain()
                        v.tensor_scalar(w8[:, 2, :], w8[:, 0, :], P - 1, None, ALU.bitwise_and)
                        v.tensor_scalar(w8[:, 3, :], w8[:, 0, :], 7, None, ALU.arith_shift_right)
                        v.drain()
                        v.tensor_tensor(binb[:, :], w8[:, 2, :], w8[:, 1, :], ALU.add)
                        v.tensor_copy(wf[:, 1, :], w8[:, 3, :])
                        v.tensor_scalar(w8[:, 4, :], w8[:, 3, :], 1.0, float(1 << KEYBITS), ALU.add, ALU.mult)
                        v.drain()
                        v.tensor_tensor(ohc[h][:, :, :], binb[:, :].unsqueeze(2).to_broadcast([P, HALF, P]),
                                        iota_p[:, :].unsqueeze(1).to_broadcast([P, HALF, P]), ALU.is_equal).then_inc(s_ohc, 1)
                        v.tensor_tensor(ohk[h][:, :, :], wf[:, 1, :].unsqueeze(2).to_broadcast([P, HALF, NBK]),
                                        iota_p[:, 0:NBK].unsqueeze(1).to_broadcast([P, HALF, NBK]), ALU.is_equal).then_inc(s_ohk, 1)
                        v.tensor_tensor(l_val[:, at], w8[:, 4, :], vals[h][:, :], ALU.bitwise_or)
                        v.tensor_tensor(wf[:, 6, :], w8[:, 4, :], vals[h][:, :], ALU.add)
                        v.tensor_copy(l_clo[:, at], binb[:, :])
                        if mark_sources:
                            v.tensor_scalar(w8[:, 5, :], vals[h][:, :], -1.0, None, ALU.add)
                            v.drain()
                            v.tensor_scalar(w8[:, 6, :], w8[:, 5, :], LO - 1, None, ALU.bitwise_and)
                            v.tensor_scalar(w8[:, 7, :], w8[:, 5, :], 5, None, ALU.arith_shift_right)
                            v.drain()
                            v.tensor_copy(wf[:, 2:4, :], w8[:, 6:8, :])
                            v.drain()
                            for c0 in range(0, HALF, 4):
                                for c in range(4):
                                    v.tensor_scalar(ohhi[:, c, :], iota_hi[:, :], wf[:, 3, c0 + c:c0 + c + 1], None, ALU.is_equal)
                                    v.tensor_scalar(ohlo[:, c, :], iota_lo[:, :], wf[:, 2, c0 + c:c0 + c + 1], None, ALU.is_equal)
                                v.drain().then_inc(s_mk, 1)
                                T_("dve", "mm").wait()

                    def rank(h, at):
                        T_("dve", "z").wait()
                        for c in range(HALF):
                            r = slice(c * P, (c + 1) * P)
                            v.scalar_tensor_tensor(rankprod[:, r], psz[:, r], 1.0, ohc[h][:, c, :], ALU.mult, ALU.mult, accum_out=wf[:, 5, c:c + 1])
                        v.drain().then_inc(s_rk, 1)
                        for c in range(HALF):
                            v.tensor_scalar(ohr0[:, c, :], iota_p[:, 0:RANKS], wf[:, 5, c:c + 1], wf[:, 6, c:c + 1], ALU.is_equal, ALU.mult)
                        v.tensor_copy(l_rank[:, at], wf[:, 5, :])
                        v.tensor_tensor(cntr[:, 0:HALF], cntr[:, 0:HALF], wf[:, 5, :], ALU.max)
                        v.drain().then_inc(s_ohr, 1)

                    v.memset(cntr[:, 0:HALF], 0.0)
                    pull(0)
                    pull(1)
                    n = v.value_load(ci[0:1, ROUNDS:ROUNDS + 1], min_val=1, max_val=T // 16)
                    with v.Fori(0, n) as i:
                        for h in range(2):
                            at = bass.ds(i * 16 + h * HALF, HALF)
                            bins(h, at)
                            pull(h)
                            rank(h, at)
                    v.drain()
                    v.tensor_reduce(cnt[:, 0:1], cntr[:, 0:HALF], AX.X, ALU.max)
                    T_("dve", "z").wait()
                    v.tensor_copy(routed[:, :], psf[:, 0, :])
                    v.tensor_reduce(cnt[:, 1:2], psd[:, 0:NBK], AX.X, ALU.max)
                    v.drain()
                    v.tensor_scalar(cnt[:, 0:1], cnt[:, 0:1], 1.0, None, ALU.add)
                    to_count(v, 0, WINDOWS, 6)
                    to_count(v, 1, PULLS, 4, 2, MAXPULLS)
                    v.tensor_scalar(ci[0:1, AHEAD:AHEAD + 1], ci[0:1, PULLS:PULLS + 1], -1.0, None, ALU.add)

                @blk.scalar
                def _(act):
                    n = act.value_load(ci[0:1, ROUNDS:ROUNDS + 1], min_val=1, max_val=T // 16)
                    with act.Fori(0, n) as _i:
                        for h in range(2):
                            T_("act", "ohc").wait()
                            nc.scalar.copy(ohcf[h], ohc[h][:, :, :].rearrange("p c b -> p (c b)")).then_inc(s_ohcf, 1)

                @blk.tensor
                def _(pe):
                    for b in range(2):
                        nc.tensor.matmul(psz[:, b * 512:(b + 1) * 512], tri[:, :], zerob[:, :], start=True, stop=False, skip_group_check=True)
                    nc.tensor.matmul(psd[:, 0:NBK], tri[:, :], zerob[:, 0:NBK], start=True, stop=False, skip_group_check=True)
                    nc.tensor.matmul(psf[:, 0, :], tri[:, :], zerob[:, :], start=True, stop=False, skip_group_check=True)
                    n = pe.value_load(ci[0:1, ROUNDS:ROUNDS + 1], min_val=1, max_val=T // 16)
                    with pe.Fori(0, n) as _i:
                        for h in range(2):
                            def add(m):
                                for b in range(2):
                                    last = nc.tensor.matmul(psz[:, b * 512:(b + 1) * 512], m[:, :],
                                                            ohc[h][:, 4 * b:4 * b + 4, :].rearrange("p c b -> p (c b)"),
                                                            start=False, stop=False, skip_group_check=True)
                                return last
                            T_("pe", "ohc").wait()
                            add(tri).then_inc(s_z, 1)
                            T_("pe", "ohk").wait()
                            for c in range(HALF):
                                nc.tensor.matmul(psd[:, 0:NBK], ohc[h][:, c, :], ohk[h][:, c, :], start=False, stop=False, skip_group_check=True)
                            if mark_sources:
                                for _k in range(2):
                                    T_("pe", "mk").wait()
                                    for c in range(4):
                                        last = nc.tensor.matmul(psm[:, 0:HI], ohlo[:, c, :], ohhi[:, c, :], start=False, stop=False, skip_group_check=True)
                                    last.then_inc(s_mm, 1)
                            T_("pe", "rk").wait()
                            add(rtri)
                            T_("pe", "ohcf").wait()
                            T_("pe", "ohr").wait()
                            for c in range(HALF):
                                nc.tensor.matmul(psf[:, 0, c * RANKS:(c + 1) * RANKS], ohcf[h][:, c * P:(c + 1) * P], ohr0[:, c, :],
                                                 start=False, stop=False, skip_group_check=True)
                    pe.drain().then_inc(s_z, 1)
                    pe_count(pe, 0)
                    pe_count(pe, 1)

        def route():
            with nc.Block() as blk:
                @blk.vector
                def _(v):
                    n = v.value_load(ci[0:1, REROUTE:REROUTE + 1], min_val=1, max_val=T // HALF)
                    with v.Fori(0, n) as i:
                        at = bass.ds(i * HALF, HALF)
                        v.tensor_scalar(wf[:, 0, :], l_rank[:, at], cnt[:, 3:4], None, ALU.subtract)
                        v.tensor_copy(wf[:, 1, :], l_clo[:, at])
                        v.tensor_scalar(w8[:, 0, :], l_val[:, at], 31 << 14, None, ALU.bitwise_and)
                        v.tensor_scalar(w8[:, 1, :], l_val[:, at], 127 << 7, None, ALU.bitwise_and)
                        v.tensor_scalar(w8[:, 2, :], l_val[:, at], 127, None, ALU.bitwise_and)
                        v.drain()
                        v.tensor_copy(wf[:, 2:5, :], w8[:, 0:3, :])
                        v.drain()
                        for c in range(HALF):
                            v.tensor_scalar(ohc[0][:, c, :], iota_p[:, :], wf[:, 1, c:c + 1], None, ALU.is_equal)
                            for q in range(3):
                                v.tensor_scalar(ohr[:, c, q, :], iota_p[:, 0:RANKS], wf[:, 0, c:c + 1], wf[:, 2 + q, c:c + 1], ALU.is_equal, ALU.mult)
                        v.drain().then_inc(s_vp, 1)
                        T_("dve", "pe").wait()
                    v.tensor_copy(routed[:, :], psd[:, :])
                    v.tensor_scalar(cnt[:, 3:4], cnt[:, 3:4], float(RANKS), None, ALU.add)

                @blk.tensor
                def _(pe):
                    nc.tensor.matmul(psd[:, :], tri[:, :], zerob[:, :], start=True, stop=False, skip_group_check=True)
                    n = pe.value_load(ci[0:1, REROUTE:REROUTE + 1], min_val=1, max_val=T // HALF)
                    with pe.Fori(0, n) as _i:
                        T_("pe", "vp").wait()
                        for c in range(HALF):
                            for q in range(3):
                                last = nc.tensor.matmul(psd[:, c * RANKS:(c + 1) * RANKS], ohc[0][:, c, :], ohr[:, c, q, :], start=False, stop=False, skip_group_check=True)
                        last.then_inc(s_pe, 1)

        def attend(table, heads, row):
            R = [rows[h][:, 0:HALF * row].rearrange("p (s r) -> p s r", r=row) for h in range(2)]
            hd = heads * D
            restart("row", s_row)
            with nc.Block() as blk:
                @blk.gpsimd
                def _(pool):
                    nb = pool.value_load(ci[0:1, BLOCKS:BLOCKS + 1], min_val=1, max_val=NBK)
                    n = pool.value_load(ci[0:1, PULLS:PULLS + 1], min_val=1, max_val=MAXPULLS)
                    with pool.Fori(0, nb) as _k:
                        with pool.Fori(0, n) as _i:
                            for h in range(2):
                                T_("pool", f"g{h}").wait()
                                for c in range(HALF):
                                    pool.indirect_dma_start(
                                        out=R[h][:, c, :], out_offset=None, in_=table,
                                        in_offset=bass.IndirectOffsetOnAxis(ap=idx[h][:, c:c + 1], axis=0)).then_inc(s_row[h], 16)
                    T_("pool", "g0").wait()

                @blk.vector
                def _(v):
                    def pull(h):
                        v.max(m8[h][:, :], block[:, :])
                        v.drain()
                        v.tensor_copy(idx[h][:, :], m8[h][:, :])
                        v.drain().then_inc(s_gi[h], 1)
                        v.match_replace(block[:, :], m8[h][:, :], block[:, :], 0.0)
                        v.drain()

                    def take(h):
                        G = R[h]
                        bc = lambda a: a[:, 0:heads].unsqueeze(1).to_broadcast([P, HALF, heads])
                        T_("dve", f"row{h}").wait()
                        v.tensor_tensor(z[:, :, 0:heads], G[:, :, D:D + heads], bc(ad), ALU.add)
                        v.drain()
                        v.scalar_tensor_tensor(z[:, :, 0:heads], z[:, :, 0:heads], SLOPE, z[:, :, 0:heads], ALU.mult, ALU.max)
                        v.drain()
                        v.tensor_reduce(red2[:, 0:heads], z[:, :, 0:heads].rearrange("p s h -> p h s"), AX.X, ALU.max)
                        v.drain()
                        v.tensor_tensor(mnew[:, 0:heads], mx[:, 0:heads], red2[:, 0:heads], ALU.max)
                        v.drain()
                        v.tensor_tensor(arg[:, 0:HALF, 0:heads], z[:, :, 0:heads], bc(mnew), ALU.subtract)
                        v.tensor_tensor(arg[:, HALF, 0:heads], mx[:, 0:heads], mnew[:, 0:heads], ALU.subtract)
                        v.drain().then_inc(s_va, 1)
                        v.tensor_copy(mx[:, 0:heads], mnew[:, 0:heads])
                        T_("dve", "ac").wait()
                        v.tensor_reduce(red2[:, 0:heads], pexp[:, 0:HALF, 0:heads].rearrange("p s h -> p h s"), AX.X, ALU.add)
                        v.tensor_tensor(den[:, 0:heads], den[:, 0:heads], pexp[:, HALF, 0:heads], ALU.mult)
                        for hh in range(heads):
                            v.tensor_tensor(wprod[:, hh * HALF * D:(hh + 1) * HALF * D].rearrange("p (s d) -> p s d", d=D), G[:, :, 0:D],
                                            pexp[:, 0:HALF, hh:hh + 1].to_broadcast([P, HALF, D]), ALU.mult)
                        v.drain()
                        v.tensor_tensor(den[:, 0:heads], den[:, 0:heads], red2[:, 0:heads], ALU.add)
                        for hh in range(heads):
                            v.tensor_reduce(wsum[:, hh * D:(hh + 1) * D], wprod[:, hh * HALF * D:(hh + 1) * HALF * D].rearrange("p (s d) -> p d s", d=D), AX.X, ALU.add)
                        v.drain()
                        for hh in range(heads):
                            r = slice(hh * D, (hh + 1) * D)
                            v.scalar_tensor_tensor(acc[:, r], acc[:, r], pexp[:, HALF, hh:hh + 1], wsum[:, r], ALU.mult, ALU.add)
                        v.drain()

                    def next_block():
                        v.tensor_scalar(block[:, :], routed[:, :], lowk[:, 0:1], 0.0, ALU.subtract, ALU.max)
                        v.drain()
                        v.scalar_tensor_tensor(block[:, :], block[:, :], float(1 << KEYBITS), block[:, :], ALU.is_lt, ALU.mult)
                        v.tensor_scalar(lowk[:, :], lowk[:, :], float(1 << KEYBITS), None, ALU.add)
                        v.drain()

                    nb = v.value_load(ci[0:1, BLOCKS:BLOCKS + 1], min_val=1, max_val=NBK)
                    n = v.value_load(ci[0:1, AHEAD:AHEAD + 1], min_val=1, max_val=MAXPULLS - 1)
                    v.memset(lowk[:, :], float(1 << KEYBITS))
                    v.drain()
                    next_block()
                    pull(0)
                    with v.Fori(0, nb) as k:
                        v.tensor_copy(ad[:, 0:heads], node_rows[:, bass.ds(k, 1), D + heads:D + 2 * heads].rearrange("p o h -> p (o h)"))
                        v.tensor_copy(mx[:, 0:heads], m_all[:, bass.ds(k, 1), 0:heads].rearrange("p o h -> p (o h)"))
                        v.tensor_copy(den[:, 0:heads], m_all[:, bass.ds(k, 1), H:H + heads].rearrange("p o h -> p (o h)"))
                        v.tensor_copy(acc[:, 0:hd], acc_all[:, bass.ds(k, 1), 0:hd].rearrange("p o h -> p (o h)"))
                        with v.Fori(0, n) as _i:
                            pull(1)
                            take(0)
                            pull(0)
                            take(1)
                        pull(1)
                        next_block()
                        take(0)
                        pull(0)
                        take(1)
                        v.tensor_copy(m_all[:, bass.ds(k, 1), 0:heads].rearrange("p o h -> p (o h)"), mx[:, 0:heads])
                        v.tensor_copy(m_all[:, bass.ds(k, 1), H:H + heads].rearrange("p o h -> p (o h)"), den[:, 0:heads])
                        v.tensor_copy(acc_all[:, bass.ds(k, 1), 0:hd].rearrange("p o h -> p (o h)"), acc[:, 0:hd])
                        v.drain()

                @blk.scalar
                def _(act):
                    nb = act.value_load(ci[0:1, BLOCKS:BLOCKS + 1], min_val=1, max_val=NBK)
                    n = act.value_load(ci[0:1, PULLS:PULLS + 1], min_val=1, max_val=MAXPULLS)
                    with act.Fori(0, nb) as _k:
                        with act.Fori(0, n) as _i:
                            for _h in range(2):
                                T_("act", "va").wait()
                                nc.scalar.activation(pexp[:, :, 0:heads], arg[:, :, 0:heads], ACT.Exp).then_inc(s_ac, 1)

        def start_nodes(heads):
            with nc.Block() as blk:
                @blk.vector
                def _(v):
                    T_("dve", "nrow").wait()
                    for hh in range(heads):
                        v.tensor_copy(acc_all[:, :, hh * D:(hh + 1) * D], node_rows[:, :, 0:D])
                    v.tensor_tensor(m_all[:, :, 0:heads], node_rows[:, :, D:D + heads], node_rows[:, :, D + heads:D + 2 * heads], ALU.add)
                    v.memset(m_all[:, :, H:H + heads], 1.0)
                    v.drain()
                    v.scalar_tensor_tensor(m_all[:, :, 0:heads], m_all[:, :, 0:heads], SLOPE, m_all[:, :, 0:heads], ALU.mult, ALU.max)

        def attend_windows(table, heads, row):
            with nc.Block() as blk:
                @blk.vector
                def _(v):
                    v.memset(cnt[:, 3:4], float(RANKS))
            W = nc.values_load(ci[0:1, WINDOWS:WINDOWS + 1], min_val=1, max_val=1 << 12)
            with nc.Fori(0, W) as _w:
                attend(table, heads, row)
                with nc.Block() as blk:
                    @blk.vector
                    def _(v):
                        v.tensor_scalar(wf[0:1, 0, 0:1], ci[0:1, WINDOWS:WINDOWS + 1], float(RANKS), cnt[0:1, 3:4], ALU.mult, ALU.is_gt)
                        v.drain()
                        v.tensor_tensor(wf[0:1, 0, 1:2], wf[0:1, 0, 0:1], ci[0:1, ROUNDS:ROUNDS + 1], ALU.mult)
                        v.drain()
                        v.tensor_scalar(ci[0:1, REROUTE:REROUTE + 1], wf[0:1, 0, 1:2], 2.0, 1.0, ALU.mult, ALU.max)
                route()

        def scatter_index(v, k):
            v.tensor_copy(wf[:, 0, 0:1], nodelist[:, bass.ds(k, 1)])
            v.drain()
            v.tensor_scalar(wf[:, 0, 1:2], wf[:, 0, 0:1], 0.0, 1.0e6, ALU.is_equal, ALU.mult)
            v.drain()
            v.tensor_tensor(sidx[:, :], wf[:, 0, 0:1], wf[:, 0, 1:2], ALU.add)

        def normalise(v, k, heads):
            v.tensor_scalar(den[:, 0:heads], m_all[:, bass.ds(k, 1), H:H + heads].rearrange("p o h -> p (o h)"), TINY, None, ALU.add)
            v.drain()
            v.reciprocal(den[:, 0:heads], den[:, 0:heads])
            v.drain()
            for hh in range(heads):
                v.tensor_scalar(acc[:, hh * D:(hh + 1) * D], acc_all[:, bass.ds(k, 1), hh * D:(hh + 1) * D].rearrange("p o h -> p (o h)"),
                                den[:, hh:hh + 1], None, ALU.mult)

        def finish1():
            with nc.Block() as blk:
                @blk.vector
                def _(v):
                    sums = m_all[:, :, H:2 * H]
                    v.tensor_scalar(sums, sums, TINY, None, ALU.add)
                    v.tensor_copy(nodef[:, :], nodelist[:, :])
                    v.drain()
                    v.reciprocal(sums, sums)
                    v.tensor_scalar(far[:, :], nodef[:, :], 0.0, 1.0e6, ALU.is_equal, ALU.mult)
                    v.drain()
                    for hh in range(H):
                        r = acc_all[:, :, hh * D:(hh + 1) * D]
                        v.tensor_tensor(r, r, m_all[:, :, H + hh:H + hh + 1].to_broadcast([P, NBK, D]), ALU.mult)
                    v.tensor_tensor(sidx_all[:, :], nodef[:, :], far[:, :], ALU.add)
                    for k0 in range(0, NBK, QB):
                        v.drain().then_inc(s_vp, 1)
                        T_("dve", "pe").wait()
                        v.tensor_copy(hT[:, :], psf[:, 0, :])
                        v.drain().then_inc(s_vp, 1)
                        T_("dve", "pe").wait()
                        v.tensor_scalar(hneg[:, :], psf[:, 1, :], b1c[:, 0:1], 0.0, ALU.add, ALU.min)
                        v.drain().then_inc(s_va, 1)
                        v.tensor_scalar(hpos[:, :], psf[:, 1, :], b1c[:, 0:1], 0.0, ALU.add, ALU.max)
                        v.drain()
                        T_("dve", "ac").wait()
                        v.scalar_tensor_tensor(hT[:, :], hneg[:, :], -1.0, hpos[:, :], ALU.add, ALU.add)
                        v.drain().then_inc(s_vp, 1)
                        T_("dve", "pe").wait()
                        v.tensor_copy(srows[:, k0:k0 + QB, :], psf[:, 2, 0:QB * ROW2].rearrange("p (k r) -> p k r", k=QB))
                        v.drain().then_inc(s_vg, 1)
                    T_("dve", "st1").wait()

                @blk.tensor
                def _(pe):
                    for k0 in range(0, NBK, QB):
                        T_("pe", "vp").wait()
                        for k in range(QB):
                            last = nc.tensor.transpose(psf[:, 0, k * P:(k + 1) * P], acc_all[:, k0 + k, :], ident[:, :])
                        last.then_inc(s_pe, 1)
                        T_("pe", "vp").wait()
                        nc.tensor.matmul(psf[:, 1, :], w1bd[:, :], hT[:, :], start=True, stop=True).then_inc(s_pe, 1)
                        T_("pe", "vp").wait()
                        for k in range(QB):
                            last = nc.tensor.matmul(psf[:, 2, k * ROW2:(k + 1) * ROW2], hT[:, k * P:(k + 1) * P], w2a[:, :], start=True, stop=True)
                        last.then_inc(s_pe, 1)

                @blk.scalar
                def _(act):
                    for _k in range(0, NBK, QB):
                        T_("act", "va").wait()
                        nc.scalar.activation(hneg[:, :], hneg[:, :], ACT.Exp).then_inc(s_ac, 1)

                @blk.gpsimd
                def _(pool):
                    for k0 in range(0, NBK, QB):
                        T_("pool", "vg").wait()
                        for k in range(k0, k0 + QB):
                            pool.indirect_dma_start(out=tab2_d, out_offset=bass.IndirectOffsetOnAxis(ap=sidx_all[:, k:k + 1], axis=0),
                                                    in_=srows[:, k, :], in_offset=None, bounds_check=N, oob_is_err=False).then_inc(s_st1, 16)

        def load_weights(eng, i):
            cols = slice(i * SCW, (i + 1) * SCW)
            for k in range(2):
                eng.dma_start(fcw[:, k, cols], fc_w[k * P:(k + 1) * P, cols]).then_inc(s_fcw, 16)
            eng.dma_start(bias[:, cols], fc_b[cols].rearrange("(o n) -> o n", o=1).to_broadcast([P, SCW])).then_inc(s_fcw, 16)

        def finish2():
            with nc.Block() as blk:
                @blk.sync
                def _(sp):
                    load_weights(sp, 0)

                @blk.vector
                def _(v):
                    nb = v.value_load(ci[0:1, BLOCKS:BLOCKS + 1], min_val=1, max_val=NBK)
                    with v.Fori(0, nb) as k:
                        normalise(v, k, 1)
                        scatter_index(v, k)
                        v.drain()
                        v.tensor_tensor(srow2[:, :], acc[:, 0:D], b2r[:, :], ALU.add)
                        v.drain().then_inc(s_vg, 1)
                        T_("dve", "st2").wait()

                @blk.gpsimd
                def _(pool):
                    nb = pool.value_load(ci[0:1, BLOCKS:BLOCKS + 1], min_val=1, max_val=NBK)
                    with pool.Fori(0, nb) as _k:
                        T_("pool", "vg").wait()
                        pool.indirect_dma_start(out=g2_d, out_offset=bass.IndirectOffsetOnAxis(ap=sidx[:, 0:1], axis=0),
                                                in_=srow2[:, :], in_offset=None, bounds_check=N, oob_is_err=False).then_inc(s_st2, 16)

        number_targets(1)
        make_words()
        filter_edges(False)
        compact_edges(True)
        with nc.Block() as blk:
            @blk.sync
            def _(sp):
                for n, a in enumerate((l_val, l_clo, l_rank)):
                    sp.dma_start(list_d[n], a).then_inc(s_list, 16)
                sp.dma_start(routed_d, routed[:, :]).then_inc(s_list, 16)
                sp.wait_ge(s_list, 64)

            @blk.vector
            def _(v):
                v.tensor_copy(nodelist2[:, :], nodelist[:, :])
                v.tensor_copy(ci2[0:1, 0:NROUNDS + 1], ci[0:1, 0:NROUNDS + 1])

        number_targets(2)
        passes = nc.values_load(ci[0:1, PASSES:PASSES + 1], min_val=1, max_val=-(-N // CAP))
        with nc.Fori(0, passes) as _pass:
            make_words()
            filter_edges(True)
            compact_edges(False)
            start_nodes(H)
            attend_windows(tab1_d, H, ROW1)
            finish1()
            with nc.Block() as blk:
                @blk.vector
                def _(v):
                    v.tensor_scalar(gs[:, :], gs[:, :], float(CAP), None, ALU.add)

        with nc.Block() as blk:
            @blk.sync
            def _(sp):
                for n, a in enumerate((l_val, l_clo, l_rank)):
                    sp.dma_start(a, list_d[n]).then_inc(s_listb, 16)
                sp.dma_start(routed[:, :], routed_d).then_inc(s_listb, 16)
                sp.wait_ge(s_listb, 64)

            @blk.vector
            def _(v):
                v.tensor_copy(nodelist[:, :], nodelist2[:, :])
                v.tensor_copy(ci[0:1, 0:NROUNDS + 1], ci2[0:1, 0:NROUNDS + 1])
                v.drain().then_inc(s_ni, 1)

            @blk.gpsimd
            def _(pool):
                pool.wait_ge(s_ni, 1)
                gather_nodes(pool, tab2_d, ROW2)

        start_nodes(1)
        attend_windows(tab2_d, 1, ROW2)
        finish2()

        with nc.Block() as blk:
            @blk.gpsimd
            def _(pool):
                for q in range(BQ):
                    pool.indirect_dma_start(out=xo[:, q, 0:D], out_offset=None, in_=user_emb,
                                            in_offset=bass.IndirectOffsetOnAxis(ap=uidx[:, q:q + 1], axis=0)).then_inc(s_user, 16)
                for q in range(BQ):
                    for c in range(CTX):
                        pool.indirect_dma_start(out=xo[:, q, (1 + c) * D:(2 + c) * D], out_offset=None, in_=g2_d,
                                                in_offset=bass.IndirectOffsetOnAxis(ap=cidx1[:, q * CTX + c:q * CTX + c + 1], axis=0)).then_inc(s_xrow, 16)

            @blk.scalar
            def _(act):
                act.wait_ge(s_xrow, 16 * BQ * CTX)
                for i in range(1, NOUT // SCW):
                    act.wait_ge(s_fcw, 48 * i)
                    load_weights(act, i)

            NC_ = SCW // NCW

            @blk.sync
            def _(sp):
                rows_out = out.rearrange("(p q) n -> q p n", q=BQ)
                with sp.Fori(0, NOUT // SCW) as i:
                    for q in range(BQ):
                        sp.wait_ge(s_staged[q % 2], i * (BQ // 2) + (q // 2 + 1))
                        sp.dma_start(rows_out[q, :, bass.ds(i * SCW, SCW)], stage[q % 2]).then_inc(s_out[q % 2], 16)
                for k in range(2):
                    sp.wait_ge(s_out[k], 16 * (1 + (NOUT // SCW) * (BQ // 2)))

            @blk.tensor
            def _(pe):
                pe.wait_ge(s_user, 16 * BQ)
                pe.wait_ge(s_xrow, 16 * BQ * CTX)
                for k in range(2):
                    for q in range(BQ):
                        last = nc.tensor.transpose(psf[:, k, q * P:(q + 1) * P], xo[:, q, k * P:(k + 1) * P], ident[:, :])
                last.then_inc(s_xt, 1)
                pe.wait_ge(s_xtc, 1)
                weights = Tally(pe, s_fcw, "pe_weights", 48, 48)
                free = Tally(pe, s_free, "pe_free", 1, 1)
                with pe.Fori(0, NOUT // SCW) as i:
                    weights.wait()
                    for q in range(BQ):
                        for c in range(NC_):
                            n = q * NC_ + c
                            bank = n % 4
                            free.wait()
                            for k in range(2):
                                last = nc.tensor.matmul(psf[:, bank, 0:NCW], xoT[:, k, q * P:(q + 1) * P],
                                                        fcw[:, k, bass.ds(i * SCW + c * NCW, NCW)], start=(k == 0), stop=(k == 1))
                            last.then_inc(s_prod, 1)

            @blk.vector
            def _(v):
                v.wait_ge(s_xt, 1)
                v.tensor_copy(xoT[:, :, :], psf[:, 0:2, :])
                v.drain().then_inc(s_xtc, 1)
                for _k in range(4):
                    v.engine_nop().then_inc(s_free, 1)
                weights = Tally(v, s_fcw, "dve_weights", 48, 48)
                done = Tally(v, s_prod, "dve_prod", 1, 1)
                for k in range(2):
                    v.engine_nop().then_inc(s_out[k], 16)
                stored = [Tally(v, s_out[k], f"dve_stored{k}", 16, 16) for k in range(2)]
                with v.Fori(0, NOUT // SCW) as i:
                    weights.wait()
                    for q in range(BQ):
                        stored[q % 2].wait()
                        for c in range(NC_):
                            done.wait()
                            n = q * NC_ + c
                            last = v.tensor_tensor(stage[q % 2][:, c * NCW:(c + 1) * NCW], psf[:, n % 4, 0:NCW],
                                                   bias[:, bass.ds(i * SCW + c * NCW, NCW)], ALU.add)
                            last.then_inc(s_free, 1)
                        v.drain().then_inc(s_staged[q % 2], 1)


_INS = ['r_user_idx', 'r_context_idx', 'L0_rec_edge_index', 'L0_rec_user_emb', 'L0_rec_service_emb', 'L0_rec_W1',
        'L0_rec_att_src1', 'L0_rec_att_dst1', 'L0_rec_b1', 'L0_rec_W2', 'L0_rec_att_src2', 'L0_rec_att_dst2',
        'L0_rec_b2', 'L0_rec_fc_w', 'L0_rec_fc_b']


def kernel(**inputs):
    import concourse.bacc as bacc
    from concourse.bass_utils import run_bass_kernel_spmd as run

    nc = bacc.Bacc("TRN2", target_bir_lowering=False, num_devices=1)
    arrays, args = {}, []
    for name in _INS:
        a = np.ascontiguousarray(inputs[name])
        arrays[f"in_{name}"] = a
        args.append(nc.dram_tensor(f"in_{name}", a.shape, mybir.dt.from_np(a.dtype), kind="ExternalInput").ap())
    rows, columns = arrays["in_r_user_idx"].shape[0], arrays["in_L0_rec_fc_w"].shape[1]
    out = nc.dram_tensor("out", [rows, columns], mybir.dt.float32, kind="ExternalOutput").ap()
    graph_kernel(nc, *args, out)
    r = run(nc, [arrays], core_ids=[0])
    return r.results[0]["out"]
```
